# Optimizing a Trainium2 kernel written in Bass

```python
import numpy as np
import jax
import jax.numpy as jnp

def _softmax(x, axis=-1):
    return jax.nn.softmax(x, axis=axis)
def _gelu(x):
    return jax.nn.gelu(x, approximate=True)
def _silu(x):
    return jax.nn.silu(x)
def _sigmoid(x):
    return jax.nn.sigmoid(x)
def _layernorm(x, axis=-1, eps=1e-5):
    m = jnp.mean(x, axis=axis, keepdims=True)
    v = jnp.var(x, axis=axis, keepdims=True)
    return (x - m) / jnp.sqrt(v + eps)
def _scatter_add(tgt, idx, src, axis=0):
    return tgt.at[idx].add(src)
def _segment_sum(src, seg, n):
    return jax.ops.segment_sum(src, seg, n)

kernel_name = 'mk_rec_standalone_d1_rec_cafcfc'

def setup_inputs(seed: int = 0):
    np.random.seed(seed)
    _w = jnp.asarray
    def _rec_inputs():
        import jax
        import jax.numpy as jnp
        _rk = jax.random.key(seed)
        r_cin_inputs = 7.22013e-05 + 1.00017 * jax.random.normal(jax.random.fold_in(_rk, 1), (1024, 32, 64), jnp.float32)
        return r_cin_inputs
    r_cin_inputs = _rec_inputs()
    def _L0_rec_setup():
        import jax, jax.numpy as jnp
        import numpy as np
        FIELD = 32
        DIM = 64
        LAYER_SIZE = (128, 128)

        def _cin(x, weights, biases):
            B, F, D = x.shape
            hidden = x
            finals = []
            n_layers = len(weights)
            for i, (w, b) in enumerate(zip(weights, biases)):
                size = w.shape[0]
                z = jnp.einsum('bhd,bfd->bhfd', hidden, x).reshape(B, hidden.shape[1] * F, D)
                y = jnp.einsum('bcd,oc->bod', z, w) + b[None, :, None]
                y = jax.nn.relu(y)
                if i != n_layers - 1:
                    hidden, direct = (y[:, :size // 2, :], y[:, size // 2:, :])
                else:
                    direct = y
                finals.append(direct)
            return jnp.concatenate(finals, axis=1).sum(-1)
        key = jax.random.key(seed)
        ks = jax.random.split(key, 5)
        B = 4096
        x = jax.random.normal(ks[0], (B, FIELD, DIM), dtype=jnp.float32)
        field_nums = [FIELD]
        params = {}
        for i, size in enumerate(LAYER_SIZE):
            in_ch = field_nums[-1] * field_nums[0]
            fan = 1.0 / np.sqrt(in_ch)
            params[f'w{i}'] = jax.random.uniform(ks[1 + 2 * i % 4], (size, in_ch), minval=-fan, maxval=fan, dtype=jnp.float32)
            params[f'b{i}'] = jax.random.uniform(ks[2 + 2 * i % 4], (size,), minval=-fan, maxval=fan, dtype=jnp.float32)
            field_nums.append(size // 2)
        return {'cin_inputs': x, 'w0': params['w0'], 'b0': params['b0'], 'w1': params['w1'], 'b1': params['b1']}
    _L0_rec_all = _L0_rec_setup()
    _L0_rec_in = {k: v for k, v in _L0_rec_all.items() if k in ('w0', 'b0', 'w1', 'b1', )}
    del _L0_rec_all

    return {
        "r_cin_inputs": r_cin_inputs,
        "L0_rec_w0": _L0_rec_in["w0"],
        "L0_rec_b0": _L0_rec_in["b0"],
        "L0_rec_w1": _L0_rec_in["w1"],
        "L0_rec_b1": _L0_rec_in["b1"],
    }

def reference(r_cin_inputs, L0_rec_w0, L0_rec_b0, L0_rec_w1, L0_rec_b1):
    import jax
    import jax.numpy as jnp
    def _L0_rec_ref(cin_inputs, w0, b0, w1, b1):
        import jax, jax.numpy as jnp
        import numpy as np
        FIELD = 32
        DIM = 64
        LAYER_SIZE = (128, 128)

        def _cin(x, weights, biases):
            B, F, D = x.shape
            hidden = x
            finals = []
            n_layers = len(weights)
            for i, (w, b) in enumerate(zip(weights, biases)):
                size = w.shape[0]
                z = jnp.einsum('bhd,bfd->bhfd', hidden, x).reshape(B, hidden.shape[1] * F, D)
                y = jnp.einsum('bcd,oc->bod', z, w) + b[None, :, None]
                y = jax.nn.relu(y)
                if i != n_layers - 1:
                    hidden, direct = (y[:, :size // 2, :], y[:, size // 2:, :])
                else:
                    direct = y
                finals.append(direct)
            return jnp.concatenate(finals, axis=1).sum(-1)
        return _cin(cin_inputs, [w0, w1], [b0, b1])

    y = _L0_rec_ref(r_cin_inputs, L0_rec_w0, L0_rec_b0, L0_rec_w1, L0_rec_b1)
    return y


_drawn_inputs = setup_inputs


def setup_inputs(seed=0):
    import zlib

    import numpy as np

    out = dict(_drawn_inputs(seed))
    spreads = {}
    factors = {}
    for name, (base, spread) in spreads.items():
        noise = np.random.default_rng([zlib.crc32(name.encode()), seed]).standard_normal(out[name].shape)
        drawn = base * np.exp(spread * noise) if base else spread * noise
        out[name] = jnp.asarray(drawn.astype(out[name].dtype))
    for name, factor in factors.items():
        out[name] = (out[name] * factor).astype(out[name].dtype)
    return out
```

```python
from contextlib import ExitStack

import concourse.bass as bass
from concourse import mybir

ALU = mybir.AluOpType
ACT = mybir.ActivationFunctionType
F32 = mybir.dt.float32
F32R = mybir.dt.float32r
AX_X = mybir.AxisListType.X

P = 128
QUAD = 32
BATCH, FIELD, DIM = 1024, 32, 64
SIZE = 128
HID = SIZE // 2
COLS = BATCH * DIM
BANK = 512
C = 2 * BANK
NCHUNK = COLS // C
BPC = C // DIM
CQ = C // 4
T1 = 4
T2 = HID * FIELD // P
LOADED = 8
NCAST = T2 - LOADED
RING = 5

CAST = [t for t in range(T2) if not 1 <= t <= LOADED]
TILE2 = [m // 2 + 1 if m % 2 == 0 else CAST[m // 2] for m in range(T2)]

L1_BEFORE = {0: 0, 2: 1, 4: 2, 6: 3}
STEPS = []
for _pos in range(T2):
    if _pos in L1_BEFORE:
        STEPS.append((1, L1_BEFORE[_pos]))
    STEPS.append((2, _pos))
STEPS1 = [s for s in STEPS if s[0] == 1]
STEPS2 = [s for s in STEPS if s[0] == 2]

KINDS = dict(zip(STEPS, "PVPPVPPVPPVPNPVPPVPN"))
POOL, DVE, NATIVE, SPLIT, ANY = "P", "V", "N", "PV", "PVN"

RELU2_AFTER, XS_AFTER, SQ_AFTER, RELU1_AFTER = 1, 2, 4, 14
RED1_AFTER, RED2_AFTER = 2, 5
SQ_BEFORE_L1 = 3
SUB_LAG = 2
LOW_LAG = 1
CAST_AHEAD = 5


class Round:

    def __init__(self, r, parity, prev=None, layer1=True, layer2=True):
        self.r, self.parity, self.prev = r, parity, prev
        self.layer1, self.layer2 = layer1, layer2
        self.steps = STEPS if layer1 and layer2 else STEPS1 if layer1 else STEPS2

    def count(self, n, kinds=ANY):
        here = sum(KINDS[s] in kinds for s in self.steps[:n])
        if not self.layer2:
            return here
        return (sum(KINDS[s] in kinds for s in STEPS1)
                + sum(KINDS[s] in kinds for s in STEPS) * self.r + here)

    def slot(self, n):
        return (n if not self.layer2 else len(STEPS1) + n) % RING

    def back(self, n, k):
        if n >= k:
            return self, n - k
        if self.prev is None:
            return None
        return self.prev.back(len(self.prev.steps) + n, k)


assert len(STEPS) % RING == 0


def rounds(eng, one_round, between=None):
    first = Round(-1, 1, layer2=False)
    one_round(first)
    if between:
        between()
    second = Round(0, 0, first)
    one_round(second)
    one_round(Round(1, 1, second))
    with eng.Fori(1, NCHUNK // 2 - 1) as pair:
        even = Round(2 * pair, 0, Round(2 * pair - 1, 1))
        one_round(even)
        one_round(Round(2 * pair + 1, 1, even))
    before = Round(NCHUNK - 2, 0, Round(NCHUNK - 3, 1))
    one_round(before)
    last = Round(NCHUNK - 1, 1, before, layer1=False)
    one_round(last)
    return last


def wait(eng, sem, value):
    if isinstance(value, int) and value <= 0:
        return
    eng.wait_ge(sem, value)


def build(nc, x2, w1a, w1b, wsq, w2, sel, bias, out_direct, out_top):
    with ExitStack() as ctx:
        def sb(name, shape, dt=F32):
            return ctx.enter_context(nc.sbuf_tensor(name, shape, dt))

        def ps(name, shape):
            return ctx.enter_context(nc.psum_tensor(name, shape, F32))

        def sem(name):
            return ctx.enter_context(nc.semaphore(name))

        x_row = sb("x_row", [P, C])
        x_rot = sb("x_rot", [P, 2, LOADED, C])
        x_pack = sb("x_pack", [P, CQ])
        xh_pack, xl_pack = sb("xh_pack", [P, CQ], F32R), sb("xl_pack", [P, CQ], F32R)
        x_parts = sb("x_parts", [P, 2, C], F32R)
        z, zh, zl = sb("z", [P, RING, C]), sb("zh", [P, RING, C], F32R), sb("zl", [P, RING, C], F32R)
        sq, sqh, sql = sb("sq", [P, CQ]), sb("sqh", [P, CQ], F32R), sb("sql", [P, CQ], F32R)
        hidden = sb("hidden", [P, 2, C])
        direct = sb("direct", [P, C // 2])
        top = sb("top", [P, C])
        sum_direct = sb("sum_direct", [P, BATCH // 2])
        sum_top = sb("sum_top", [P, BATCH])
        w1h, w1l = sb("w1h", [P, T1, SIZE], F32R), sb("w1l", [P, T1, SIZE], F32R)
        w2h, w2l = sb("w2h", [P, T2, SIZE], F32R), sb("w2l", [P, T2, SIZE], F32R)
        wqh, wql = sb("wqh", [P, 4, SIZE], F32R), sb("wql", [P, 4, SIZE], F32R)
        natives = [k for layer, k in STEPS2 if KINDS[layer, k] == NATIVE]
        assert all(KINDS[s] != NATIVE for s in STEPS1)
        w2n = sb("w2n", [P, max(1, len(natives)), SIZE])
        select = sb("select", [P, NCAST, P], F32R)
        biases = sb("biases", [P, 2])
        raw_w2 = x_rot[:, 1, 0:2, :].rearrange("p a (t o) -> p (a t) o", o=SIZE)
        raw_w1a = x_rot[:, 1, 2, 0:T1 * SIZE].rearrange("p (t o) -> p t o", o=SIZE)
        raw_w1b = x_rot[:, 1, 3, 0:T1 * SIZE].rearrange("p (t o) -> p t o", o=SIZE)
        raw_wsq = x_rot[:, 1, 4, 0:4 * SIZE].rearrange("p (g o) -> p g o", o=SIZE)
        raw_sel = x_rot[:, 1, 5, :].rearrange("p (t o) -> p t o", o=P)
        folded_w1 = x_rot[:, 1, 6, 0:T1 * SIZE].rearrange("p (t o) -> p t o", o=SIZE)

        y1 = ps("y1", [P, C])
        y2 = ps("y2", [P, C])
        cast = ps("cast", [P, 2, C])

        s_weights1 = sem("s_weights1")
        s_weights2 = sem("s_weights2")
        s_folded = sem("s_folded")
        s_w1high = sem("s_w1high")
        s_w1low = sem("s_w1low")
        s_w2high = sem("s_w2high")
        s_w2low = sem("s_w2low")
        s_row = sem("s_row")
        s_pack = sem("s_pack")
        s_rot = [[sem(f"s_rot{par}_{t}") for t in range(LOADED)] for par in range(2)]
        s_zero = sem("s_zero")
        s_xh = sem("s_xh")
        s_xl = sem("s_xl")
        s_parts = sem("s_parts")
        s_cast = sem("s_cast")
        s_prod = sem("s_prod")
        s_high = sem("s_high")
        s_low = {POOL: sem("s_low_pool"), DVE: sem("s_low_dve")}
        s_mmhigh = sem("s_mmhigh")
        s_mmlow = sem("s_mmlow")
        s_sq = sem("s_sq")
        s_sql = sem("s_sql")
        s_sqmm = sem("s_sqmm")
        s_hidden = sem("s_hidden")
        s_direct = sem("s_direct")
        s_top = sem("s_top")
        s_red1 = sem("s_red1")
        s_red2 = sem("s_red2")
        s_out = sem("s_out")
        s_carry = sem("s_carry")

        W1_HIGH, W2_HIGH = 2, 2 + len(natives)

        def rows_of_x(col, quadrant_step, first, width):
            at = x2[first:first + 1, bass.ds(col, C)]
            return bass.AP(at.tensor, at.offset, [[quadrant_step, 4], [COLS, QUAD], [1, width]])

        def subtract(eng, R, n):
            who = KINDS[R.steps[n]]
            eng.wait_ge(s_high, R.count(n + 1, SPLIT))
            used = R.back(n, RING)
            if used:
                wait(eng, s_mmlow, used[0].count(used[1] + 1, SPLIT))
            eng.tensor_tensor(zl[:, R.slot(n), :], z[:, R.slot(n), :], zh[:, R.slot(n), :].bitcast(F32),
                              ALU.subtract).then_inc(s_low[who], 1)

        block = ctx.enter_context(nc.Block())

        @block.sync
        def _(sp):
            def load_row(n):
                sp.dma_start(x_row[:, :], rows_of_x(n * C, 4 * COLS, 0, C)).then_inc(s_row, 16)

            def load_pack(n):
                sp.dma_start(x_pack[:, :], rows_of_x(n * C, CQ, 0, CQ)).then_inc(s_pack, 16)

            def load_rot(n, par, t):
                sp.dma_start(x_rot[:, par, t - 1, :], rows_of_x(n * C, 8 * COLS, t, C))\
                  .then_inc(s_rot[par][t - 1], 16)

            def unpack(n, par):
                carry(s_xl, n + 1)
                if not isinstance(n, int) or n >= 2:
                    carry(s_cast, NCAST * (n - 1))
                for quad, pack in enumerate((xh_pack, xl_pack)):
                    for g in range(4):
                        part = x_parts[quad * QUAD:(quad + 1) * QUAD, par, g * CQ:(g + 1) * CQ]
                        sp.dma_start(part.bitcast(F32), pack[g * QUAD:(g + 1) * QUAD, :].bitcast(F32))\
                          .then_inc(s_parts, 16)

            def carry(sem, value):
                sp.wait_ge(sem, value)
                sp.sem_inc(s_carry, 1)

            load_row(0)
            load_rot(0, 0, 1)
            sp.dma_start(raw_w1a, w1a).then_inc(s_weights1, 16)
            sp.dma_start(raw_w1b, w1b).then_inc(s_weights1, 16)
            load_pack(0)
            sp.dma_start(raw_wsq, wsq).then_inc(s_weights1, 16)
            sp.dma_start(biases[:, :], bias).then_inc(s_weights1, 16)
            for t in range(2, T1 + 1):
                load_rot(0, 0, t)
            sp.dma_start(raw_sel, sel).then_inc(s_weights2, 16)
            sp.dma_start(raw_w2, w2).then_inc(s_weights2, 16)
            sp.wait_ge(s_zero, 1)
            unpack(0, 0)
            for t in range(T1 + 1, LOADED + 1):
                load_rot(0, 0, t)

            def one_round(R):
                for n, (layer, k) in enumerate(R.steps):
                    if layer == 2 and k % 2 == 0 and R.layer1 and not is_late(R):
                        carry(s_prod, R.count(n + 1))
                        load_rot(R.r + 2, R.parity, TILE2[k])
                    if n == SQ_AFTER + 1 and R.layer1 and R.layer2:
                        unpack(R.r + 1, 1 - R.parity)
                        if not is_late(R):
                            carry(s_sq, 2 * (R.r + 2))
                            load_pack(R.r + 2)
                    if layer == 1 and k == T1 - 1 and not is_late(R):
                        carry(s_prod, R.count(n + 1))
                        load_row(R.r + 2)

            def is_late(R):
                return isinstance(R.r, int) and R.r + 2 >= NCHUNK

            def second_chunk():
                sp.wait_ge(s_w1low, 2)
                sp.wait_ge(s_w2high, W2_HIGH)
                sp.wait_ge(s_w2low, 1)
                for t in range(1, LOADED + 1):
                    load_rot(1, 1, t)
                carry(s_sq, 2)
                load_pack(1)

            rounds(sp, one_round, second_chunk)
            sp.wait_ge(s_red1, NCHUNK)
            sp.dma_start(out_direct, sum_direct[:, :]).then_inc(s_out, 16)
            sp.wait_ge(s_red2, NCHUNK)
            sp.dma_start(out_top, sum_top[:, :]).then_inc(s_out, 16)
            sp.wait_ge(s_out, 32)

        @block.tensor
        def _(pe):
            def spread(R, k):
                chunk, m = R.r, k // 2
                if m == 0:
                    pe.wait_ge(s_parts, 8 * 16 * (chunk + 1))
                Q, pos = (R, k - 4) if k >= 4 else (R.prev, T2 + k - 4)
                if Q.layer2:
                    pe.wait_ge(s_prod, Q.count(Q.steps.index((2, pos)) + 1))
                for h in range(2):
                    mm = pe.matmul(cast[:, m % 2, h * BANK:(h + 1) * BANK], select[:, m, :],
                                   x_parts[:, R.parity, h * BANK:(h + 1) * BANK], start=True, stop=True)
                mm.then_inc(s_cast, 1)

            def high_part(R, n):
                step = layer, k = R.steps[n]
                if k == 0 and layer == 1:
                    wait(pe, s_hidden, 2 * (R.r + 1))
                    wait(pe, s_direct, 2 * (R.r + 1))
                if k == 0 and layer == 2:
                    wait(pe, s_top, R.r)
                if KINDS[step] == NATIVE:
                    pe.wait_ge(s_prod, R.count(n + 1))
                    y, last = (y2, k == T2 - 1)
                    for h in range(2):
                        mm = pe.matmul(y[:, h * BANK:(h + 1) * BANK], w2n[:, natives.index(k), :],
                                       z[:, R.slot(n), h * BANK:(h + 1) * BANK],
                                       start=False, stop=last, skip_group_check=True)
                else:
                    y, wh, wl = (y1, w1h, w1l) if layer == 1 else (y2, w2h, w2l)
                    pe.wait_ge(s_high, R.count(n + 1, SPLIT))
                    for w in (wl, wh):
                        for h in range(2):
                            mm = pe.matmul(y[:, h * BANK:(h + 1) * BANK], w[:, k, :],
                                           zh[:, R.slot(n), h * BANK:(h + 1) * BANK],
                                           start=k == 0 and w is wl, stop=False, skip_group_check=True)
                mm.then_inc(s_mmhigh, 1)

            def low_part(R, n):
                step = layer, k = R.steps[n]
                y, wh = (y1, w1h) if layer == 1 else (y2, w2h)
                pe.wait_ge(s_low[KINDS[step]], R.count(n + 1, KINDS[step]))
                for h in range(2):
                    mm = pe.matmul(y[:, h * BANK:(h + 1) * BANK], wh[:, k, :],
                                   zl[:, R.slot(n), h * BANK:(h + 1) * BANK],
                                   start=False, stop=k == (T1 if layer == 1 else T2) - 1,
                                   skip_group_check=True)
                mm.then_inc(s_mmlow, 1)

            def squares(n):
                pe.wait_ge(s_sql, n + 1)
                for w, part in ((wql, sqh), (wqh, sqh), (wqh, sql)):
                    for g in range(4):
                        mm = pe.matmul(y1[:, g * CQ:(g + 1) * CQ], w[:, g, :], part[:, :],
                                       start=False, stop=False, skip_group_check=True)
                mm.then_inc(s_sqmm, 1)

            def selections(R, n):
                at = n + CAST_AHEAD
                if at >= len(R.steps):
                    if not R.layer1:
                        return
                    nxt = next_round(R)
                    at -= len(R.steps)
                    if at < len(nxt.steps) and nxt.steps[at][0] == 2 and nxt.steps[at][1] % 2:
                        spread(nxt, nxt.steps[at][1])
                elif R.steps[at][0] == 2 and R.steps[at][1] % 2:
                    spread(R, R.steps[at][1])

            def next_round(R):
                last = isinstance(R.r, int) and R.r == NCHUNK - 2
                return Round(R.r + 1, 1 - R.parity, R, layer1=not last)

            def one_round(R):
                for n, step in enumerate(R.steps):
                    if R.layer2:
                        selections(R, n)
                    if step == (1, SQ_BEFORE_L1):
                        squares(R.r + 1)
                    behind = R.back(n, LOW_LAG)
                    behind = behind and KINDS[behind[0].steps[behind[1]]] != NATIVE \
                        and (behind[0] is R or behind[0].layer2) and behind
                    if behind and KINDS[step] == NATIVE:
                        low_part(*behind)
                    high_part(R, n)
                    if behind and KINDS[step] != NATIVE:
                        low_part(*behind)
                if not R.layer2:
                    low_part(R, len(R.steps) - 1)

            def first_selections():
                pe.wait_ge(s_w2high, W2_HIGH)
                pe.wait_ge(s_w2low, 1)
                first = Round(0, 0, Round(-1, 1, layer2=False))
                for layer, k in first.steps[:CAST_AHEAD]:
                    if layer == 2 and k % 2:
                        spread(first, k)

            pe.wait_ge(s_w1high, W1_HIGH)
            pe.wait_ge(s_w1low, 2)
            rounds(pe, one_round, first_selections)

        @block.scalar
        def _(act):
            def relu_top(R):
                act.wait_ge(s_mmhigh, R.count(len(R.steps)))
                wait(act, s_red2, R.r)
                act.activation(top[:, :], y2[:, :], ACT.Relu, bias=biases[:, 1:2]).then_inc(s_top, 1)

            def relu_layer1(R):
                n, par = R.r + 1, 1 - R.parity
                act.wait_ge(s_mmlow, R.count(R.steps.index((1, T1 - 1)) + 1, SPLIT))
                if R.prev is not None and R.layer2:
                    act.wait_ge(s_prod, R.prev.count(len(R.prev.steps)))
                for half in range(2):
                    act.activation(hidden[half * HID:(half + 1) * HID, par, :], y1[0:HID, :],
                                   ACT.Relu, bias=biases[0:HID, 0:1]).then_inc(s_hidden, 1)
                wait(act, s_red1, n)
                for half in range(2):
                    act.activation(direct[half * HID:(half + 1) * HID, :],
                                   y1[HID:P, half * BANK:(half + 1) * BANK],
                                   ACT.Relu, bias=biases[HID:P, 0:1]).then_inc(s_direct, 1)

            def split_x(n):
                act.wait_ge(s_pack, 16 * (n + 1))
                wait(act, s_parts, 8 * 16 * n)
                act.activation(xh_pack[:, :], x_pack[:, :], ACT.Copy).then_inc(s_xh, 1)

            def square(n):
                act.wait_ge(s_pack, 16 * (n + 1))
                wait(act, s_sqmm, n)
                act.activation(sq[:, :], x_pack[:, :], ACT.Square).then_inc(s_sq, 1)
                act.activation(sqh[:, :], x_pack[:, :], ACT.Square).then_inc(s_sq, 1)

            def one_round(R):
                for n, step in enumerate(R.steps):
                    if KINDS[step] != NATIVE:
                        act.wait_ge(s_prod, R.count(n + 1))
                        used = R.back(n, RING)
                        if used:
                            act.wait_ge(s_mmhigh, used[0].count(used[1] + 1))
                        act.activation(zh[:, R.slot(n), :], z[:, R.slot(n), :], ACT.Copy)\
                           .then_inc(s_high, 1)
                    if n == RELU2_AFTER and R.layer2 and R.prev.layer2:
                        relu_top(R.prev)
                    if n == XS_AFTER and R.layer1 and R.layer2:
                        split_x(R.r + 1)
                    if n == SQ_AFTER and R.layer1 and R.layer2:
                        square(R.r + 1)
                    if n == RELU1_AFTER and R.layer1:
                        relu_layer1(R)
                if not R.layer2:
                    relu_layer1(R)

            act.wait_ge(s_weights1, 64)
            act.activation(wqh[:, :, :], raw_wsq, ACT.Copy).then_inc(s_w1high, 1)
            act.wait_ge(s_folded, 1)
            act.activation(w1h[:, :, :], folded_w1, ACT.Copy).then_inc(s_w1high, 1)
            split_x(0)
            square(0)

            def second_weights():
                act.wait_ge(s_weights2, 32)
                act.activation(select[:, :, :], raw_sel, ACT.Copy).then_inc(s_w2high, 1)
                act.activation(w2h[:, :, :], raw_w2, ACT.Copy).then_inc(s_w2high, 1)
                for n, k in enumerate(natives):
                    act.activation(w2n[:, n, :], raw_w2[:, k, :], ACT.Copy).then_inc(s_w2high, 1)

            second_weights()
            relu_top(rounds(act, one_round))

        @block.gpsimd
        def _(pool):
            def low_x(n):
                pool.wait_ge(s_xh, n + 1)
                pool.tensor_tensor(xl_pack[:, :], x_pack[:, :], xh_pack[:, :].bitcast(F32),
                                   ALU.subtract).then_inc(s_xl, 1)

            def low_square(n):
                pool.wait_ge(s_sq, 2 * (n + 1))
                pool.tensor_tensor(sql[:, :], sq[:, :], sqh[:, :].bitcast(F32),
                                   ALU.subtract).then_inc(s_sql, 1)

            def one_round(R):
                for n, step in enumerate(R.steps):
                    if KINDS[step] == POOL:
                        subtract(pool, R, n)
                    if n == XS_AFTER and R.layer1 and R.layer2:
                        low_x(R.r + 1)
                    if n == SQ_AFTER and R.layer1 and R.layer2:
                        low_square(R.r + 1)

            pool.memset(x_parts[:, :, :].bitcast(F32), 0.0).then_inc(s_zero, 1)
            low_x(0)
            low_square(0)
            rounds(pool, one_round)

        @block.vector
        def _(dve):
            def loads(R, ahead):
                if isinstance(R.r, int):
                    return 16 * ((R.r + ahead) // 2 + 1)
                return 8 * (R.r - R.parity) + 16 * ((R.parity + ahead) // 2 + 1)

            def product(R, n):
                layer, k = R.steps[n]
                used = R.back(n, RING)
                if used:
                    Q, m = used
                    who = KINDS[Q.steps[m]]
                    if who == NATIVE:
                        dve.wait_ge(s_mmhigh, Q.count(m + 1))
                    else:
                        dve.wait_ge(s_low[who], Q.count(m + 1, who))
                if layer == 1:
                    par = 1 - R.parity
                    if k == 0:
                        dve.wait_ge(s_row, 16 * (R.r + 2))
                    dve.wait_ge(s_rot[par][k], loads(R, 1))
                    row, x = x_row[:, :], x_rot[:, par, k, :]
                else:
                    if k == 0:
                        dve.wait_ge(s_hidden, 2 * (R.r + 1))
                    if k % 2:
                        dve.wait_ge(s_cast, NCAST * R.r + k // 2 + 1)
                        x = cast[:, (k // 2) % 2, :]
                    else:
                        if TILE2[k] > T1:
                            dve.wait_ge(s_rot[R.parity][TILE2[k] - 1], loads(R, 0))
                        x = x_rot[:, R.parity, TILE2[k] - 1, :]
                    row = hidden[:, R.parity, :]
                dve.tensor_tensor(z[:, R.slot(n), :], row, x, ALU.mult).then_inc(s_prod, 1)

            def reduce_direct(R):
                dve.wait_ge(s_direct, 2 * (R.r + 1))
                dve.tensor_reduce(sum_direct[:, bass.ds(R.r * (BPC // 2), BPC // 2)],
                                  direct[:, :].rearrange("p (b d) -> p b d", d=DIM), AX_X, ALU.add)\
                   .then_inc(s_red1, 1)

            def reduce_top(R):
                dve.wait_ge(s_top, R.r + 1)
                dve.tensor_reduce(sum_top[:, bass.ds(R.r * BPC, BPC)],
                                  top[:, :].rearrange("p (b d) -> p b d", d=DIM), AX_X, ALU.add)\
                   .then_inc(s_red2, 1)

            def one_round(R):
                for n in range(len(R.steps)):
                    product(R, n)
                    behind = R.back(n, SUB_LAG)
                    if behind and KINDS[behind[0].steps[behind[1]]] == DVE:
                        subtract(dve, *behind)
                    if R.layer2 and n == RED1_AFTER:
                        reduce_direct(R)
                    if R.layer2 and R.prev.layer2 and n == RED2_AFTER:
                        reduce_top(R.prev)

            dve.wait_ge(s_weights1, 64)
            dve.tensor_tensor(folded_w1, raw_w1a, raw_w1b, ALU.add).then_inc(s_folded, 1)
            dve.wait_ge(s_w1high, W1_HIGH)
            dve.wait_ge(s_folded, 1)
            dve.tensor_tensor(w1l[:, :, :], folded_w1, w1h[:, :, :].bitcast(F32),
                              ALU.subtract).then_inc(s_w1low, 1)
            dve.tensor_tensor(wql[:, :, :], raw_wsq, wqh[:, :, :].bitcast(F32),
                              ALU.subtract).then_inc(s_w1low, 1)
            dve.wait_ge(s_w2high, W2_HIGH)
            dve.tensor_tensor(w2l[:, :, :], raw_w2, w2h[:, :, :].bitcast(F32),
                              ALU.subtract).then_inc(s_w2low, 1)

            last = rounds(dve, one_round)
            reduce_top(last)


def kernel(r_cin_inputs, L0_rec_w0, L0_rec_b0, L0_rec_w1, L0_rec_b1):
    import numpy as np
    import concourse.bacc as bacc
    from concourse.bass_utils import run_bass_kernel_spmd

    x = np.asarray(r_cin_inputs)
    rows = np.ascontiguousarray(x.transpose(1, 0, 2)).reshape(FIELD, COLS)
    x2 = np.concatenate([rows, rows], axis=0)

    p = np.arange(P)
    q, i = p // QUAD, p % QUAD
    w0 = np.asarray(L0_rec_w0).reshape(SIZE, FIELD, FIELD)
    t1 = np.arange(1, T1 + 1)
    row_field = np.broadcast_to((i + 4 * q) % FIELD, (T1, P))
    rot_field = (i[None] + t1[:, None] + 8 * q[None]) % FIELD
    w1a = w0[:, row_field, rot_field].transpose(2, 1, 0)
    w1b = w0[:, rot_field, row_field].transpose(2, 1, 0).copy()
    w1b[3 * QUAD:, T1 - 1, :] = 0
    wsq = np.zeros((P, 4, SIZE), np.float32)
    wsq[p, q] = w0[:, i, i].T
    w1 = np.asarray(L0_rec_w1).reshape(SIZE, HID, FIELD)
    t2 = np.array(TILE2)
    w2 = w1[:, np.broadcast_to(p % HID, (T2, P)), (i[None] + t2[:, None] + 8 * q[None]) % FIELD]
    w2 = w2.transpose(2, 1, 0)
    sel = np.zeros((P, NCAST, P), np.float32)
    for m, t in enumerate(CAST):
        f = (i + t + 8 * q) % FIELD
        sel[f, m, p] = 1
        sel[QUAD + f, m, p] = 1
    bias = np.stack([np.asarray(L0_rec_b0), np.asarray(L0_rec_b1)], axis=1)

    arrays = {"x2": x2, "w1a": w1a, "w1b": w1b, "wsq": wsq, "w2": w2, "sel": sel, "bias": bias}
    arrays = {k: np.ascontiguousarray(v) for k, v in arrays.items()}
    nc = bacc.Bacc("TRN2", target_bir_lowering=False, num_devices=1)
    args = [nc.dram_tensor(k, v.shape, mybir.dt.from_np(v.dtype), kind="ExternalInput").ap()
            for k, v in arrays.items()]
    out_direct = nc.dram_tensor("out_direct", (P, BATCH // 2), F32, kind="ExternalOutput").ap()
    out_top = nc.dram_tensor("out_top", (P, BATCH), F32, kind="ExternalOutput").ap()
    build(nc, *args, out_direct, out_top)
    got = run_bass_kernel_spmd(nc, [arrays], core_ids=[0]).results[0]
    direct = np.asarray(got["out_direct"]).reshape(2, HID, NCHUNK, BPC // 2).transpose(2, 0, 3, 1)
    direct = direct.reshape(BATCH, HID)
    return np.ascontiguousarray(np.concatenate([direct, np.asarray(got["out_top"]).T], axis=1))
```

```python
from contextlib import ExitStack

import concourse.bass as bass
from concourse import mybir

ALU = mybir.AluOpType
ACT = mybir.ActivationFunctionType
F32 = mybir.dt.float32
F32R = mybir.dt.float32r
AX_X = mybir.AxisListType.X

P = 128
QUAD = 32
BATCH, FIELD, DIM = 1024, 32, 64
SIZE = 128
HID = SIZE // 2
COLS = BATCH * DIM
BANK = 512
C = 2 * BANK
NCHUNK = COLS // C
BPC = C // DIM
CQ = C // 4
T1 = 4
T2 = HID * FIELD // P
NROT = 8
XROWS = NROT - 1 + 3 * 8 + FIELD
RING = 5

ORDER = "12122221222122222222"
KIND_OF = "VNVNPNPVNPPVNPPVNNPN"
STEPS = [(int(a), ORDER[:n].count(a)) for n, a in enumerate(ORDER)]
STEPS1 = [s for s in STEPS if s[0] == 1]
STEPS2 = [s for s in STEPS if s[0] == 2]
KINDS = dict(zip(STEPS, KIND_OF))
POOL, DVE, NATIVE, SPLIT, ANY = "P", "V", "N", "PV", "PVN"

SWAP = T2 // 2
TILE2 = [k if k < SWAP else (k + 1) % NROT for k in range(T2)]
TILE1 = [k + 1 for k in range(T1)]
SPLIT2 = [k for layer, k in STEPS2 if KINDS[layer, k] != NATIVE]
NATIVE2 = [k for layer, k in STEPS2 if KINDS[layer, k] == NATIVE]
NSPLIT2 = len(SPLIT2)
assert len(STEPS1) == T1 and len(STEPS2) == T2 and SWAP == NROT

RELU2_AFTER, SQ_AFTER, COPY_SWAPPED_AFTER, RELU1_AFTER, COPY_HIDDEN_AFTER = 1, 4, 2, 15, 16
RED1_AFTER, RED2_AFTER = 1, 5
SQ_BEFORE_L1 = 3
SUB_LAG = 2
POOL_BEHIND = 0
assert STEPS.index((2, SWAP - 1)) <= COPY_HIDDEN_AFTER
LOW_LAG = 1


class Round:

    def __init__(self, r, parity, prev=None, layer1=True, layer2=True):
        self.r, self.parity, self.prev = r, parity, prev
        self.layer1, self.layer2 = layer1, layer2
        self.steps = STEPS if layer1 and layer2 else STEPS1 if layer1 else STEPS2

    def count(self, n, kinds=ANY):
        here = sum(KINDS[s] in kinds for s in self.steps[:n])
        if not self.layer2:
            return here
        return (sum(KINDS[s] in kinds for s in STEPS1)
                + sum(KINDS[s] in kinds for s in STEPS) * self.r + here)

    def slot(self, n):
        return (n if not self.layer2 else len(STEPS1) + n) % RING

    def back(self, n, k):
        if n >= k:
            return self, n - k
        if self.prev is None:
            return None
        return self.prev.back(len(self.prev.steps) + n, k)


assert len(STEPS) % RING == 0


def rounds(eng, one_round, between=None):
    first = Round(-1, 1, layer2=False)
    one_round(first)
    if between:
        between()
    second = Round(0, 0, first)
    one_round(second)
    one_round(Round(1, 1, second))
    with eng.Fori(1, NCHUNK // 2 - 1) as pair:
        even = Round(2 * pair, 0, Round(2 * pair - 1, 1))
        one_round(even)
        one_round(Round(2 * pair + 1, 1, even))
    before = Round(NCHUNK - 2, 0, Round(NCHUNK - 3, 1))
    one_round(before)
    last = Round(NCHUNK - 1, 1, before, layer1=False)
    one_round(last)
    return last


def wait(eng, sem, value):
    if isinstance(value, int) and value <= 0:
        return
    eng.wait_ge(sem, value)


def build(nc, x2, w1a, w1b, wsq, w2, bias, out_direct, out_top):
    with ExitStack() as ctx:
        def sb(name, shape, dt=F32):
            return ctx.enter_context(nc.sbuf_tensor(name, shape, dt))

        def ps(name, shape):
            return ctx.enter_context(nc.psum_tensor(name, shape, F32))

        def sem(name):
            return ctx.enter_context(nc.semaphore(name))

        x_row = sb("x_row", [P, C])
        x_rot = sb("x_rot", [P, 2, NROT, C])
        x_pack = sb("x_pack", [P, CQ])
        z, zh, zl = sb("z", [P, RING, C]), sb("zh", [P, RING, C], F32R), sb("zl", [P, RING, C], F32R)
        sq, sqh, sql = sb("sq", [P, CQ]), sb("sqh", [P, CQ], F32R), sb("sql", [P, CQ], F32R)
        hidden = sb("hidden", [P, C])
        swapped = sb("swapped", [P, C])
        direct = sb("direct", [P, C // 2])
        top = sb("top", [P, C])
        sum_direct = sb("sum_direct", [P, BATCH // 2])
        sum_top = sb("sum_top", [P, BATCH])
        w1h, w1l = sb("w1h", [P, T1, SIZE], F32R), sb("w1l", [P, T1, SIZE], F32R)
        w2h, w2l = sb("w2h", [P, NSPLIT2, SIZE], F32R), sb("w2l", [P, NSPLIT2, SIZE], F32R)
        wqh, wql = sb("wqh", [P, 4, SIZE], F32R), sb("wql", [P, 4, SIZE], F32R)
        assert all(KINDS[s] != NATIVE for s in STEPS1)
        w2n = sb("w2n", [P, len(NATIVE2), SIZE])
        biases = sb("biases", [P, 2])
        raw_w2 = x_rot[:, 1, 6:8, :].rearrange("p a (t o) -> p (a t) o", o=SIZE)
        raw_w1 = x_rot[:, 1, 0, :].rearrange("p (a t o) -> p a t o", a=2, o=SIZE)
        raw_w1a, raw_w1b = raw_w1[:, 0], raw_w1[:, 1]
        raw_wsq = x_rot[:, 1, 5, 0:4 * SIZE].rearrange("p (g o) -> p g o", o=SIZE)
        folded_w1 = x_rot[:, 1, 5, C - T1 * SIZE:C].rearrange("p (t o) -> p t o", o=SIZE)

        y1 = ps("y1", [P, C])
        y2 = ps("y2", [P, C])
        hidden_ps = ps("hidden_ps", [P, C])
        swapped_ps = ps("swapped_ps", [P, C])

        s_weights1 = sem("s_weights1")
        s_weights2 = sem("s_weights2")
        s_folded = sem("s_folded")
        s_w1high = sem("s_w1high")
        s_w1low = sem("s_w1low")
        s_w2high = sem("s_w2high")
        s_w2low = sem("s_w2low")
        s_row = sem("s_row")
        s_pack = sem("s_pack")
        s_rot = [[sem(f"s_rot{par}_{t}") for t in range(NROT)] for par in range(2)]
        s_prod = sem("s_prod")
        s_high = sem("s_high")
        s_low = {POOL: sem("s_low_pool"), DVE: sem("s_low_dve")}
        s_mmhigh = sem("s_mmhigh")
        s_mmlow = sem("s_mmlow")
        s_sq = sem("s_sq")
        s_sql = sem("s_sql")
        s_sqmm = sem("s_sqmm")
        s_hidden = sem("s_hidden")
        s_swapped = sem("s_swapped")
        s_hidden_ps = sem("s_hidden_ps")
        s_swapped_ps = sem("s_swapped_ps")
        s_direct = sem("s_direct")
        s_top = sem("s_top")
        s_red1 = sem("s_red1")
        s_red2 = sem("s_red2")
        s_out = sem("s_out")
        s_carry = sem("s_carry")

        W1_HIGH, W2_HIGH = 2, 2

        def rows_of_x(n, quadrant_step, first=0, width=C):
            at = x2[bass.ds(n * XROWS + first, 1), :]
            return bass.AP(at.tensor, at.offset, [[quadrant_step, 4], [C, QUAD], [1, width]])

        def subtract(eng, R, n):
            who = KINDS[R.steps[n]]
            eng.wait_ge(s_high, R.count(n + 1, SPLIT))
            used = R.back(n, RING)
            if used:
                wait(eng, s_mmlow, used[0].count(used[1] + 1, SPLIT))
            eng.tensor_tensor(zl[:, R.slot(n), :], z[:, R.slot(n), :], zh[:, R.slot(n), :].bitcast(F32),
                              ALU.subtract).then_inc(s_low[who], 1)

        block = ctx.enter_context(nc.Block())

        @block.sync
        def _(sp):
            def load_row(n):
                sp.dma_start(x_row[:, :], rows_of_x(n, 4 * C)).then_inc(s_row, 16)

            def load_pack(n):
                sp.dma_start(x_pack[:, :], rows_of_x(n, CQ, width=CQ)).then_inc(s_pack, 16)

            def load_rot(n, par, t):
                sp.dma_start(x_rot[:, par, t, :], rows_of_x(n, 8 * C, first=t))\
                  .then_inc(s_rot[par][t], 16)

            def swap(R):
                carry(s_hidden, 2 * (R.r + 2))
                if R.layer2:
                    carry(s_swapped_ps, R.r + 1)
                sp.dma_start(swapped[QUAD:P, :], hidden[0:P - QUAD, :]).then_inc(s_swapped, 16)
                sp.dma_start(swapped[0:QUAD, :], hidden[P - QUAD:P, :]).then_inc(s_swapped, 16)

            def carry(sem, value):
                sp.wait_ge(sem, value)
                sp.sem_inc(s_carry, 1)

            load_row(0)
            load_rot(0, 0, 1)
            sp.dma_start(raw_w1a, w1a).then_inc(s_weights1, 16)
            sp.dma_start(raw_w1b, w1b).then_inc(s_weights1, 16)
            load_pack(0)
            sp.dma_start(raw_wsq, wsq).then_inc(s_weights1, 16)
            sp.dma_start(biases[:, :], bias).then_inc(s_weights1, 16)
            for t in range(2, T1 + 1):
                load_rot(0, 0, t)
            sp.dma_start(raw_w2, w2).then_inc(s_weights2, 16)
            for t in [0] + list(range(T1 + 1, NROT)):
                load_rot(0, 0, t)

            def one_round(R):
                for n, (layer, k) in enumerate(R.steps):
                    if layer == 2 and k >= SWAP and not is_late(R):
                        carry(s_prod, R.count(n + 1))
                        load_rot(R.r + 2, R.parity, TILE2[k])
                    if n == SQ_AFTER + 1 and R.layer1 and R.layer2 and not is_late(R):
                        carry(s_sq, 2 * (R.r + 2))
                        load_pack(R.r + 2)
                    if layer == 1 and k == T1 - 1 and not is_late(R):
                        carry(s_prod, R.count(n + 1))
                        load_row(R.r + 2)
                    if n == RELU1_AFTER and R.layer1:
                        swap(R)

            def is_late(R):
                return isinstance(R.r, int) and R.r + 2 >= NCHUNK

            def second_chunk():
                for t in TILE1:
                    load_rot(1, 1, t)
                carry(s_sq, 2)
                load_pack(1)
                swap(Round(-1, 1, layer2=False))
                sp.wait_ge(s_w1low, 2)
                load_rot(1, 1, 0)
                load_rot(1, 1, 5)
                sp.wait_ge(s_w2high, W2_HIGH)
                sp.wait_ge(s_w2low, 1)
                load_rot(1, 1, 6)
                load_rot(1, 1, 7)

            rounds(sp, one_round, second_chunk)
            sp.wait_ge(s_red1, NCHUNK)
            sp.dma_start(out_direct, sum_direct[:, :]).then_inc(s_out, 16)
            sp.wait_ge(s_red2, NCHUNK)
            sp.dma_start(out_top, sum_top[:, :]).then_inc(s_out, 16)
            sp.wait_ge(s_out, 32)

        @block.tensor
        def _(pe):
            def high_part(R, n):
                step = layer, k = R.steps[n]
                if k == 0 and layer == 1:
                    wait(pe, s_hidden, 2 * (R.r + 1))
                    wait(pe, s_direct, 2 * (R.r + 1))
                if k == 0 and layer == 2:
                    wait(pe, s_top, R.r)
                if KINDS[step] == NATIVE:
                    pe.wait_ge(s_prod, R.count(n + 1))
                    y, last = (y2, k == T2 - 1)
                    for h in range(2):
                        mm = pe.matmul(y[:, h * BANK:(h + 1) * BANK], w2n[:, NATIVE2.index(k), :],
                                       z[:, R.slot(n), h * BANK:(h + 1) * BANK],
                                       start=k == 0, stop=last, skip_group_check=True)
                else:
                    y, wh, wl = (y1, w1h, w1l) if layer == 1 else (y2, w2h, w2l)
                    at = k if layer == 1 else SPLIT2.index(k)
                    pe.wait_ge(s_high, R.count(n + 1, SPLIT))
                    for w in (wl, wh):
                        for h in range(2):
                            mm = pe.matmul(y[:, h * BANK:(h + 1) * BANK], w[:, at, :],
                                           zh[:, R.slot(n), h * BANK:(h + 1) * BANK],
                                           start=k == 0 and w is wl, stop=False, skip_group_check=True)
                mm.then_inc(s_mmhigh, 1)

            def low_part(R, n):
                step = layer, k = R.steps[n]
                y, wh, at = (y1, w1h, k) if layer == 1 else (y2, w2h, SPLIT2.index(k))
                pe.wait_ge(s_low[KINDS[step]], R.count(n + 1, KINDS[step]))
                for h in range(2):
                    mm = pe.matmul(y[:, h * BANK:(h + 1) * BANK], wh[:, at, :],
                                   zl[:, R.slot(n), h * BANK:(h + 1) * BANK],
                                   start=False, stop=k == (T1 if layer == 1 else T2) - 1,
                                   skip_group_check=True)
                mm.then_inc(s_mmlow, 1)

            def squares(n):
                pe.wait_ge(s_sql, n + 1)
                for w, part in ((wql, sqh), (wqh, sqh), (wqh, sql)):
                    for g in range(4):
                        mm = pe.matmul(y1[:, g * CQ:(g + 1) * CQ], w[:, g, :], part[:, :],
                                       start=False, stop=False, skip_group_check=True)
                mm.then_inc(s_sqmm, 1)

            def one_round(R):
                for n, step in enumerate(R.steps):
                    if step == (1, SQ_BEFORE_L1):
                        squares(R.r + 1)
                    behind = R.back(n, LOW_LAG)
                    behind = behind and KINDS[behind[0].steps[behind[1]]] != NATIVE \
                        and (behind[0] is R or behind[0].layer2) and behind
                    if behind and KINDS[step] == NATIVE:
                        low_part(*behind)
                    high_part(R, n)
                    if behind and KINDS[step] != NATIVE:
                        low_part(*behind)
                if not R.layer2:
                    low_part(R, len(R.steps) - 1)

            def second_weights():
                pe.wait_ge(s_w2high, W2_HIGH)
                pe.wait_ge(s_w2low, 1)

            pe.wait_ge(s_w1high, W1_HIGH)
            pe.wait_ge(s_w1low, 2)
            rounds(pe, one_round, second_weights)

        @block.scalar
        def _(act):
            def relu_top(R):
                act.wait_ge(s_mmhigh, R.count(len(R.steps)))
                wait(act, s_red2, R.r)
                act.activation(top[:, :], y2[:, :], ACT.Relu, bias=biases[:, 1:2]).then_inc(s_top, 1)

            def relu_layer1(R):
                n = R.r + 1
                act.wait_ge(s_mmlow, R.count(R.steps.index((1, T1 - 1)) + 1, SPLIT))
                if R.layer2:
                    act.wait_ge(s_swapped, 32 * n)
                    act.wait_ge(s_hidden_ps, n)
                for half in range(2):
                    act.activation(hidden[half * HID:(half + 1) * HID, :], y1[0:HID, :],
                                   ACT.Relu, bias=biases[0:HID, 0:1]).then_inc(s_hidden, 1)
                wait(act, s_red1, n)
                for half in range(2):
                    act.activation(direct[half * HID:(half + 1) * HID, :],
                                   y1[HID:P, half * BANK:(half + 1) * BANK],
                                   ACT.Relu, bias=biases[HID:P, 0:1]).then_inc(s_direct, 1)

            def copy_hidden(R):
                act.wait_ge(s_hidden, 2 * (R.r + 2))
                if R.layer2:
                    act.wait_ge(s_prod, R.count(R.steps.index((2, SWAP - 1)) + 1))
                act.activation(hidden_ps[:, :], hidden[:, :], ACT.Copy).then_inc(s_hidden_ps, 1)

            def copy_swapped(R):
                act.wait_ge(s_swapped, 32 * (R.r + 1))
                if R.prev.layer2:
                    act.wait_ge(s_prod, R.prev.count(len(R.prev.steps)))
                act.activation(swapped_ps[:, :], swapped[:, :], ACT.Copy).then_inc(s_swapped_ps, 1)

            def square(n):
                act.wait_ge(s_pack, 16 * (n + 1))
                wait(act, s_sqmm, n)
                act.activation(sq[:, :], x_pack[:, :], ACT.Square).then_inc(s_sq, 1)
                act.activation(sqh[:, :], x_pack[:, :], ACT.Square).then_inc(s_sq, 1)

            def second_weights():
                act.wait_ge(s_weights2, 16)
                act.activation(w2h[:, :, :], raw_w2[:, :NSPLIT2, :], ACT.Copy).then_inc(s_w2high, 1)
                act.activation(w2n[:, :, :], raw_w2[:, NSPLIT2:, :], ACT.Copy).then_inc(s_w2high, 1)

            def one_round(R):
                for n, step in enumerate(R.steps):
                    if KINDS[step] != NATIVE:
                        act.wait_ge(s_prod, R.count(n + 1))
                        used = R.back(n, RING)
                        if used:
                            act.wait_ge(s_mmhigh, used[0].count(used[1] + 1))
                        act.activation(zh[:, R.slot(n), :], z[:, R.slot(n), :], ACT.Copy)\
                           .then_inc(s_high, 1)
                    if n == RELU2_AFTER and R.layer2 and R.prev.layer2:
                        relu_top(R.prev)
                    if n == COPY_SWAPPED_AFTER and R.layer2:
                        copy_swapped(R)
                    if n == SQ_AFTER and R.layer1 and R.layer2:
                        square(R.r + 1)
                    if n == RELU1_AFTER and R.layer1:
                        relu_layer1(R)
                    if n == COPY_HIDDEN_AFTER and R.layer1:
                        copy_hidden(R)
                if not R.layer2:
                    second_weights()
                    relu_layer1(R)
                    copy_hidden(R)

            act.wait_ge(s_weights1, 64)
            act.activation(wqh[:, :, :], raw_wsq, ACT.Copy).then_inc(s_w1high, 1)
            act.wait_ge(s_folded, 1)
            act.activation(w1h[:, :, :], folded_w1, ACT.Copy).then_inc(s_w1high, 1)
            square(0)

            relu_top(rounds(act, one_round))

        @block.gpsimd
        def _(pool):
            def low_square(n):
                pool.wait_ge(s_sq, 2 * (n + 1))
                pool.tensor_tensor(sql[:, :], sq[:, :], sqh[:, :].bitcast(F32),
                                   ALU.subtract).then_inc(s_sql, 1)

            def one_round(R):
                for n, step in enumerate(R.steps):
                    if KINDS[step] == POOL:
                        if n + POOL_BEHIND < len(R.steps):
                            pool.wait_ge(s_prod, R.count(n + 1 + POOL_BEHIND))
                        subtract(pool, R, n)
                    if n == SQ_AFTER and R.layer1 and R.layer2:
                        low_square(R.r + 1)

            low_square(0)
            rounds(pool, one_round)

        @block.vector
        def _(dve):
            def loads(R, ahead):
                if isinstance(R.r, int):
                    return 16 * ((R.r + ahead) // 2 + 1)
                return 8 * (R.r - R.parity) + 16 * ((R.parity + ahead) // 2 + 1)

            def product(R, n):
                layer, k = R.steps[n]
                used = R.back(n, RING)
                if used:
                    Q, m = used
                    who = KINDS[Q.steps[m]]
                    if who == NATIVE:
                        dve.wait_ge(s_mmhigh, Q.count(m + 1))
                    else:
                        dve.wait_ge(s_low[who], Q.count(m + 1, who))
                if layer == 1:
                    par = 1 - R.parity
                    if k == 0:
                        dve.wait_ge(s_row, 16 * (R.r + 2))
                    t = TILE1[k]
                    dve.wait_ge(s_rot[par][t], loads(R, 1))
                    row, x = x_row[:, :], x_rot[:, par, t, :]
                else:
                    if k == 0:
                        dve.wait_ge(s_hidden_ps, R.r + 1)
                    if k == SWAP:
                        dve.wait_ge(s_swapped_ps, R.r + 1)
                    t = TILE2[k]
                    if t not in TILE1 and k < SWAP:
                        dve.wait_ge(s_rot[R.parity][t], loads(R, 0))
                    row, x = hidden_ps if k < SWAP else swapped_ps, x_rot[:, R.parity, t, :]
                    row = row[:, :]
                dve.tensor_tensor(z[:, R.slot(n), :], row, x, ALU.mult).then_inc(s_prod, 1)

            def reduce_direct(R):
                dve.wait_ge(s_direct, 2 * (R.r + 1))
                dve.tensor_reduce(sum_direct[:, bass.ds(R.r * (BPC // 2), BPC // 2)],
                                  direct[:, :].rearrange("p (b d) -> p b d", d=DIM), AX_X, ALU.add)\
                   .then_inc(s_red1, 1)

            def reduce_top(R):
                dve.wait_ge(s_top, R.r + 1)
                dve.tensor_reduce(sum_top[:, bass.ds(R.r * BPC, BPC)],
                                  top[:, :].rearrange("p (b d) -> p b d", d=DIM), AX_X, ALU.add)\
                   .then_inc(s_red2, 1)

            def one_round(R):
                for n in range(len(R.steps)):
                    product(R, n)
                    behind = R.back(n, SUB_LAG)
                    if behind and KINDS[behind[0].steps[behind[1]]] == DVE \
                            and (behind[0] is R or behind[0].layer2):
                        subtract(dve, *behind)
                    if R.layer2 and n == RED1_AFTER:
                        reduce_direct(R)
                    if R.layer2 and R.prev.layer2 and n == RED2_AFTER:
                        reduce_top(R.prev)
                if not R.layer2:
                    for n in range(len(R.steps) - SUB_LAG, len(R.steps)):
                        if KINDS[R.steps[n]] == DVE:
                            subtract(dve, R, n)

            dve.wait_ge(s_weights1, 64)
            dve.tensor_tensor(folded_w1, raw_w1a, raw_w1b, ALU.add).then_inc(s_folded, 1)
            dve.wait_ge(s_w1high, W1_HIGH)
            dve.wait_ge(s_folded, 1)
            dve.tensor_tensor(w1l[:, :, :], folded_w1, w1h[:, :, :].bitcast(F32),
                              ALU.subtract).then_inc(s_w1low, 1)
            dve.tensor_tensor(wql[:, :, :], raw_wsq, wqh[:, :, :].bitcast(F32),
                              ALU.subtract).then_inc(s_w1low, 1)
            def second_weights():
                dve.wait_ge(s_w2high, W2_HIGH)
                dve.tensor_tensor(w2l[:, :, :], raw_w2[:, :NSPLIT2, :], w2h[:, :, :].bitcast(F32),
                                  ALU.subtract).then_inc(s_w2low, 1)

            last = rounds(dve, one_round, second_weights)
            reduce_top(last)


def kernel(r_cin_inputs, L0_rec_w0, L0_rec_b0, L0_rec_w1, L0_rec_b1):
    import numpy as np
    import concourse.bacc as bacc
    from concourse.bass_utils import run_bass_kernel_spmd

    x = np.asarray(r_cin_inputs)
    rows = np.ascontiguousarray(x.transpose(1, 0, 2)).reshape(FIELD, COLS)
    x2 = rows[np.arange(XROWS) % FIELD].reshape(XROWS, NCHUNK, C).transpose(1, 0, 2)
    x2 = np.ascontiguousarray(x2).reshape(NCHUNK * XROWS, C)

    p = np.arange(P)
    q, i = p // QUAD, p % QUAD
    w0 = np.asarray(L0_rec_w0).reshape(SIZE, FIELD, FIELD)
    t1 = np.arange(1, T1 + 1)
    row_field = np.broadcast_to((i + 4 * q) % FIELD, (T1, P))
    rot_field = (i[None] + t1[:, None] + 8 * q[None]) % FIELD
    w1a = w0[:, row_field, rot_field].transpose(2, 1, 0)
    w1b = w0[:, rot_field, row_field].transpose(2, 1, 0).copy()
    w1b[3 * QUAD:, T1 - 1, :] = 0
    wsq = np.zeros((P, 4, SIZE), np.float32)
    wsq[p, q] = w0[:, i, i].T
    w1 = np.asarray(L0_rec_w1).reshape(SIZE, HID, FIELD)
    k2 = np.array(SPLIT2 + NATIVE2)[:, None]
    t2 = np.array(TILE2)[k2]
    swap = QUAD * (k2 >= SWAP)
    w2 = w1[:, (p + swap) % HID, (i + t2 + 8 * q) % FIELD]
    w2 = w2.transpose(2, 1, 0)
    bias = np.stack([np.asarray(L0_rec_b0), np.asarray(L0_rec_b1)], axis=1)

    arrays = {"x2": x2, "w1a": w1a, "w1b": w1b, "wsq": wsq, "w2": w2, "bias": bias}
    arrays = {k: np.ascontiguousarray(v) for k, v in arrays.items()}
    nc = bacc.Bacc("TRN2", target_bir_lowering=False, num_devices=1)
    args = [nc.dram_tensor(k, v.shape, mybir.dt.from_np(v.dtype), kind="ExternalInput").ap()
            for k, v in arrays.items()]
    out_direct = nc.dram_tensor("out_direct", (P, BATCH // 2), F32, kind="ExternalOutput").ap()
    out_top = nc.dram_tensor("out_top", (P, BATCH), F32, kind="ExternalOutput").ap()
    build(nc, *args, out_direct, out_top)
    got = run_bass_kernel_spmd(nc, [arrays], core_ids=[0]).results[0]
    direct = np.asarray(got["out_direct"]).reshape(2, HID, NCHUNK, BPC // 2).transpose(2, 0, 3, 1)
    direct = direct.reshape(BATCH, HID)
    return np.ascontiguousarray(np.concatenate([direct, np.asarray(got["out_top"]).T], axis=1))
```

```python
from contextlib import ExitStack

import concourse.bass as bass
from concourse import mybir

ALU = mybir.AluOpType
ACT = mybir.ActivationFunctionType
F32 = mybir.dt.float32
F32R = mybir.dt.float32r
AX_X = mybir.AxisListType.X

P = 128
QUAD = 32
BATCH, FIELD, DIM = 1024, 32, 64
SIZE = 128
HID = SIZE // 2
COLS = BATCH * DIM
BANK = 512
C = 2 * BANK
NCHUNK = COLS // C
BPC = C // DIM
T1 = 4
T2 = HID * FIELD // P
NROT = 8
XROWS = NROT - 1 + 3 * 8 + FIELD
RING = 5

ORDER = "12122221222122222222"
KIND_OF = "VNVNPNPVNPPVNPPPNNPN"
STEPS = [(int(a), ORDER[:n].count(a)) for n, a in enumerate(ORDER)]
STEPS1 = [s for s in STEPS if s[0] == 1]
STEPS2 = [s for s in STEPS if s[0] == 2]
KINDS = dict(zip(STEPS, KIND_OF))
POOL, DVE, NATIVE, SPLIT, ANY = "P", "V", "N", "PV", "PVN"

SWAP = T2 // 2
TILE2 = [k % NROT for k in range(T2)]
TILE1 = [k + 1 for k in range(T1)]
SPLIT2 = [k for layer, k in STEPS2 if KINDS[layer, k] != NATIVE]
NATIVE2 = [k for layer, k in STEPS2 if KINDS[layer, k] == NATIVE]
NSPLIT2 = len(SPLIT2)
assert len(STEPS1) == T1 and len(STEPS2) == T2 and SWAP == NROT

RELU2_AFTER, SQ_AFTER, COPY_SWAPPED_AFTER, RELU1_AFTER, COPY_HIDDEN_AFTER = 2, 4, 2, 15, 15
RED1_AFTER, RED2_AFTER = 0, 4
SQ_BEFORE_L1 = 3
SUB_LAG = 2
assert STEPS.index((2, SWAP - 1)) <= COPY_HIDDEN_AFTER
LOW_LAG = {DVE: 1, POOL: 2}
assert KINDS[STEPS[-1]] == NATIVE and STEPS[-1] == (2, T2 - 1)


class Round:

    def __init__(self, r, parity, prev=None, layer1=True, layer2=True):
        self.r, self.parity, self.prev = r, parity, prev
        self.layer1, self.layer2 = layer1, layer2
        self.steps = STEPS if layer1 and layer2 else STEPS1 if layer1 else STEPS2

    def count(self, n, kinds=ANY):
        here = sum(KINDS[s] in kinds for s in self.steps[:n])
        if not self.layer2:
            return here
        return (sum(KINDS[s] in kinds for s in STEPS1)
                + sum(KINDS[s] in kinds for s in STEPS) * self.r + here)

    def lows_at(self, n):
        place, places = 0, []
        for m, step in enumerate(self.steps):
            if KINDS[step] in SPLIT:
                place = max(place, m + LOW_LAG[KINDS[step]])
                places.append((m, min(place, len(self.steps) - self.layer2)))
        return [m for m, at in places if at == n]

    def loads(self, ahead):
        if isinstance(self.r, int):
            return 16 * ((self.r + ahead) // 2 + 1)
        return 8 * (self.r - self.parity) + 16 * ((self.parity + ahead) // 2 + 1)

    def slot(self, n):
        return (n if not self.layer2 else len(STEPS1) + n) % RING

    def back(self, n, k):
        if n >= k:
            return self, n - k
        if self.prev is None:
            return None
        return self.prev.back(len(self.prev.steps) + n, k)


assert len(STEPS) % RING == 0


def rounds(eng, one_round, between=None):
    first = Round(-1, 1, layer2=False)
    one_round(first)
    if between:
        between()
    second = Round(0, 0, first)
    one_round(second)
    one_round(Round(1, 1, second))
    with eng.Fori(1, NCHUNK // 2 - 1) as pair:
        even = Round(2 * pair, 0, Round(2 * pair - 1, 1))
        one_round(even)
        one_round(Round(2 * pair + 1, 1, even))
    before = Round(NCHUNK - 2, 0, Round(NCHUNK - 3, 1))
    one_round(before)
    last = Round(NCHUNK - 1, 1, before, layer1=False)
    one_round(last)
    return last


def wait(eng, sem, value):
    if isinstance(value, int) and value <= 0:
        return
    eng.wait_ge(sem, value)


def build(nc, x2, w1a, w1b, wsq, w2, bias, out_direct, out_top):
    with ExitStack() as ctx:
        def sb(name, shape, dt=F32):
            return ctx.enter_context(nc.sbuf_tensor(name, shape, dt))

        def ps(name, shape):
            return ctx.enter_context(nc.psum_tensor(name, shape, F32))

        def sem(name):
            return ctx.enter_context(nc.semaphore(name))

        x_row = sb("x_row", [P, C])
        x_rot = sb("x_rot", [P, 2, NROT, C])
        z, zh, zl = sb("z", [P, RING, C]), sb("zh", [P, RING, C], F32R), sb("zl", [P, RING, C], F32R)
        sq, sq_parts = sb("sq", [QUAD, C]), sb("sq_parts", [P, C], F32R)
        hidden = sb("hidden", [P, C])
        swapped = sb("swapped", [P, C])
        direct = sb("direct", [P, C // 2])
        top = sb("top", [P, C])
        sum_direct = sb("sum_direct", [P, BATCH // 2])
        sum_top = sb("sum_top", [P, BATCH])
        w1h, w1l = sb("w1h", [P, T1, SIZE], F32R), sb("w1l", [P, T1, SIZE], F32R)
        w2h, w2l = sb("w2h", [P, NSPLIT2, SIZE], F32R), sb("w2l", [P, NSPLIT2, SIZE], F32R)
        wq = sb("wq", [P, SIZE], F32R)
        assert all(KINDS[s] != NATIVE for s in STEPS1)
        w2n = sb("w2n", [P, len(NATIVE2), SIZE])
        biases = sb("biases", [P, 2])
        raw_w2 = x_rot[:, 1, 6:8, :].rearrange("p a (t o) -> p (a t) o", o=SIZE)
        raw_w1 = x_rot[:, 1, 0, :].rearrange("p (a t o) -> p a t o", a=2, o=SIZE)
        raw_w1a, raw_w1b = raw_w1[:, 0], raw_w1[:, 1]
        raw_wsq = x_rot[:, 1, 5, 0:SIZE]
        folded_w1 = x_rot[:, 1, 5, C - T1 * SIZE:C].rearrange("p (t o) -> p t o", o=SIZE)

        y1 = ps("y1", [P, C])
        y2 = ps("y2", [P, C])
        hidden_ps = ps("hidden_ps", [P, C])
        swapped_ps = ps("swapped_ps", [P, C])

        s_weights1 = sem("s_weights1")
        s_weights2 = sem("s_weights2")
        s_folded = sem("s_folded")
        s_w1high = sem("s_w1high")
        s_w1low = sem("s_w1low")
        s_w2high = sem("s_w2high")
        s_w2low = sem("s_w2low")
        s_row = sem("s_row")
        s_rot = [[sem(f"s_rot{par}_{t}") for t in range(NROT)] for par in range(2)]
        s_prod = sem("s_prod")
        s_high = sem("s_high")
        s_low = {POOL: sem("s_low_pool"), DVE: sem("s_low_dve")}
        s_mmhigh = sem("s_mmhigh")
        s_mmlow = sem("s_mmlow")
        s_sq = sem("s_sq")
        s_sql = sem("s_sql")
        s_sqmm = sem("s_sqmm")
        s_hidden = sem("s_hidden")
        s_swapped = sem("s_swapped")
        s_hidden_ps = sem("s_hidden_ps")
        s_swapped_ps = sem("s_swapped_ps")
        s_direct = sem("s_direct")
        s_top = sem("s_top")
        s_red1 = sem("s_red1")
        s_red2 = sem("s_red2")
        s_out = sem("s_out")
        s_carry = sem("s_carry")

        W1_HIGH, W2_HIGH = 2, 2

        def rows_of_x(n, quadrant_step, first=0, width=C):
            at = x2[bass.ds(n * XROWS + first, 1), :]
            return bass.AP(at.tensor, at.offset, [[quadrant_step, 4], [C, QUAD], [1, width]])

        def subtract(eng, R, n):
            who = KINDS[R.steps[n]]
            eng.wait_ge(s_high, R.count(n + 1, SPLIT))
            used = R.back(n, RING)
            if used:
                wait(eng, s_mmlow, used[0].count(used[1] + 1, SPLIT))
            eng.tensor_tensor(zl[:, R.slot(n), :], z[:, R.slot(n), :], zh[:, R.slot(n), :].bitcast(F32),
                              ALU.subtract).then_inc(s_low[who], 1)

        block = ctx.enter_context(nc.Block())

        @block.sync
        def _(sp):
            def load_row(n):
                sp.dma_start(x_row[:, :], rows_of_x(n, 4 * C)).then_inc(s_row, 16)

            def load_rot(n, par, t):
                sp.dma_start(x_rot[:, par, t, :], rows_of_x(n, 8 * C, first=t))\
                  .then_inc(s_rot[par][t], 16)

            def swap(R):
                carry(s_hidden, 2 * (R.r + 2))
                if R.layer2:
                    carry(s_swapped_ps, R.r + 1)
                sp.dma_start(swapped[QUAD:P, :], hidden[0:P - QUAD, :]).then_inc(s_swapped, 16)
                sp.dma_start(swapped[0:QUAD, :], hidden[P - QUAD:P, :]).then_inc(s_swapped, 16)

            def carry(sem, value):
                sp.wait_ge(sem, value)
                sp.sem_inc(s_carry, 1)

            load_row(0)
            load_rot(0, 0, 1)
            sp.dma_start(raw_w1a, w1a).then_inc(s_weights1, 16)
            sp.dma_start(raw_w1b, w1b).then_inc(s_weights1, 16)
            load_rot(0, 0, 0)
            sp.dma_start(raw_wsq, wsq).then_inc(s_weights1, 16)
            sp.dma_start(biases[:, :], bias).then_inc(s_weights1, 16)
            for t in range(2, T1 + 1):
                load_rot(0, 0, t)
            sp.dma_start(raw_w2, w2).then_inc(s_weights2, 16)
            for t in range(T1 + 1, NROT):
                load_rot(0, 0, t)

            def one_round(R):
                for n, (layer, k) in enumerate(R.steps):
                    if layer == 2 and k >= SWAP and not is_late(R):
                        carry(s_prod, R.count(n + 1))
                        if TILE2[k] == 0:
                            carry(s_sq, 2 * (R.r + 1))
                        load_rot(R.r + 2, R.parity, TILE2[k])
                    if layer == 1 and k == T1 - 1 and not is_late(R):
                        carry(s_prod, R.count(n + 1))
                        load_row(R.r + 2)
                    if n == RELU1_AFTER and R.layer1:
                        swap(R)

            def is_late(R):
                return isinstance(R.r, int) and R.r + 2 >= NCHUNK

            def second_chunk():
                for t in TILE1:
                    load_rot(1, 1, t)
                sp.wait_ge(s_w1low, 2)
                load_rot(1, 1, 0)
                swap(Round(-1, 1, layer2=False))
                load_rot(1, 1, 5)
                sp.wait_ge(s_w2high, W2_HIGH)
                sp.wait_ge(s_w2low, 1)
                load_rot(1, 1, 6)
                load_rot(1, 1, 7)

            rounds(sp, one_round, second_chunk)
            sp.wait_ge(s_red1, NCHUNK)
            sp.dma_start(out_direct, sum_direct[:, :]).then_inc(s_out, 16)
            sp.wait_ge(s_red2, NCHUNK)
            sp.dma_start(out_top, sum_top[:, :]).then_inc(s_out, 16)
            sp.wait_ge(s_out, 32)

        @block.tensor
        def _(pe):
            def high_part(R, n):
                step = layer, k = R.steps[n]
                if k == 0 and layer == 1:
                    wait(pe, s_hidden, 2 * (R.r + 1))
                    wait(pe, s_direct, 2 * (R.r + 1))
                if k == 0 and layer == 2:
                    wait(pe, s_top, R.r)
                if KINDS[step] == NATIVE:
                    pe.wait_ge(s_prod, R.count(n + 1))
                    y, last = (y2, k == T2 - 1)
                    for h in range(2):
                        mm = pe.matmul(y[:, h * BANK:(h + 1) * BANK], w2n[:, NATIVE2.index(k), :],
                                       z[:, R.slot(n), h * BANK:(h + 1) * BANK],
                                       start=k == 0, stop=last, skip_group_check=True)
                else:
                    y, wh, wl = (y1, w1h, w1l) if layer == 1 else (y2, w2h, w2l)
                    at = k if layer == 1 else SPLIT2.index(k)
                    pe.wait_ge(s_high, R.count(n + 1, SPLIT))
                    for w in (wl, wh):
                        for h in range(2):
                            mm = pe.matmul(y[:, h * BANK:(h + 1) * BANK], w[:, at, :],
                                           zh[:, R.slot(n), h * BANK:(h + 1) * BANK],
                                           start=k == 0 and w is wl, stop=False, skip_group_check=True)
                mm.then_inc(s_mmhigh, 1)

            def low_part(R, n):
                step = layer, k = R.steps[n]
                y, wh, at = (y1, w1h, k) if layer == 1 else (y2, w2h, SPLIT2.index(k))
                pe.wait_ge(s_low[KINDS[step]], R.count(n + 1, KINDS[step]))
                for h in range(2):
                    mm = pe.matmul(y[:, h * BANK:(h + 1) * BANK], wh[:, at, :],
                                   zl[:, R.slot(n), h * BANK:(h + 1) * BANK],
                                   start=False, stop=k == (T1 if layer == 1 else T2) - 1,
                                   skip_group_check=True)
                mm.then_inc(s_mmlow, 1)

            def squares(n):
                pe.wait_ge(s_sql, n + 1)
                for h in range(2):
                    mm = pe.matmul(y1[:, h * BANK:(h + 1) * BANK], wq[:, :],
                                   sq_parts[:, h * BANK:(h + 1) * BANK],
                                   start=False, stop=False, skip_group_check=True)
                mm.then_inc(s_sqmm, 1)

            def one_round(R):
                for n, step in enumerate(R.steps):
                    if step == (1, SQ_BEFORE_L1):
                        squares(R.r + 1)
                    if KINDS[step] != NATIVE:
                        high_part(R, n)
                    for m in R.lows_at(n):
                        low_part(R, m)
                    if KINDS[step] == NATIVE:
                        high_part(R, n)
                for m in R.lows_at(len(R.steps)):
                    low_part(R, m)

            def second_weights():
                pe.wait_ge(s_w2high, W2_HIGH)
                pe.wait_ge(s_w2low, 1)

            pe.wait_ge(s_w1high, W1_HIGH)
            pe.wait_ge(s_w1low, 2)
            rounds(pe, one_round, second_weights)

        @block.scalar
        def _(act):
            def relu_top(R):
                act.wait_ge(s_mmhigh, R.count(len(R.steps)))
                wait(act, s_red2, R.r)
                act.activation(top[:, :], y2[:, :], ACT.Relu, bias=biases[:, 1:2]).then_inc(s_top, 1)

            def relu_layer1(R):
                n = R.r + 1
                act.wait_ge(s_mmlow, R.count(R.steps.index((1, T1 - 1)) + 1, SPLIT))
                if R.layer2:
                    act.wait_ge(s_swapped, 32 * n)
                    act.wait_ge(s_hidden_ps, n)
                for half in range(2):
                    act.activation(hidden[half * HID:(half + 1) * HID, :], y1[0:HID, :],
                                   ACT.Relu, bias=biases[0:HID, 0:1]).then_inc(s_hidden, 1)
                wait(act, s_red1, n)
                for half in range(2):
                    act.activation(direct[half * HID:(half + 1) * HID, :],
                                   y1[HID:P, half * BANK:(half + 1) * BANK],
                                   ACT.Relu, bias=biases[HID:P, 0:1]).then_inc(s_direct, 1)

            def copy_hidden(R):
                act.wait_ge(s_hidden, 2 * (R.r + 2))
                if R.layer2:
                    act.wait_ge(s_prod, R.count(R.steps.index((2, SWAP - 1)) + 1))
                act.activation(hidden_ps[:, :], hidden[:, :], ACT.Copy).then_inc(s_hidden_ps, 1)

            def copy_swapped(R):
                act.wait_ge(s_swapped, 32 * (R.r + 1))
                if R.prev.layer2:
                    act.wait_ge(s_prod, R.prev.count(len(R.prev.steps)))
                act.activation(swapped_ps[:, :], swapped[:, :], ACT.Copy).then_inc(s_swapped_ps, 1)

            def square(n, par, loaded):
                act.wait_ge(s_rot[par][0], loaded)
                wait(act, s_sqmm, n)
                act.activation(sq_parts[:, :], x_rot[:, par, 0, :], ACT.Square).then_inc(s_sq, 1)
                act.activation(sq[:, :], x_rot[0:QUAD, par, 0, :], ACT.Square).then_inc(s_sq, 1)

            def second_weights():
                act.wait_ge(s_weights2, 16)
                act.activation(w2h[:, :, :], raw_w2[:, :NSPLIT2, :], ACT.Copy).then_inc(s_w2high, 1)
                act.activation(w2n[:, :, :], raw_w2[:, NSPLIT2:, :], ACT.Copy).then_inc(s_w2high, 1)

            def one_round(R):
                for n, step in enumerate(R.steps):
                    if KINDS[step] != NATIVE:
                        act.wait_ge(s_prod, R.count(n + 1))
                        used = R.back(n, RING)
                        if used:
                            act.wait_ge(s_mmhigh, used[0].count(used[1] + 1))
                        act.activation(zh[:, R.slot(n), :], z[:, R.slot(n), :], ACT.Copy)\
                           .then_inc(s_high, 1)
                    if n == RELU2_AFTER and R.layer2 and R.prev.layer2:
                        relu_top(R.prev)
                    if n == COPY_SWAPPED_AFTER and R.layer2:
                        copy_swapped(R)
                    if n == SQ_AFTER and R.layer1 and R.layer2:
                        square(R.r + 1, 1 - R.parity, R.loads(1))
                    if n == RELU1_AFTER and R.layer1:
                        relu_layer1(R)
                    if n == COPY_HIDDEN_AFTER and R.layer1:
                        copy_hidden(R)
                if not R.layer2:
                    second_weights()
                    relu_layer1(R)
                    copy_hidden(R)

            act.wait_ge(s_weights1, 64)
            act.activation(wq[:, :], raw_wsq, ACT.Copy).then_inc(s_w1high, 1)
            act.wait_ge(s_folded, 1)
            act.activation(w1h[:, :, :], folded_w1, ACT.Copy).then_inc(s_w1high, 1)
            square(0, 0, 16)

            relu_top(rounds(act, one_round))

        @block.gpsimd
        def _(pool):
            def low_square(n):
                pool.wait_ge(s_sq, 2 * (n + 1))
                part = sq_parts[0:QUAD, :]
                pool.tensor_tensor(part, sq[:, :], part.bitcast(F32), ALU.subtract)\
                    .then_inc(s_sql, 1)

            def one_round(R):
                for n, step in enumerate(R.steps):
                    if KINDS[step] == POOL:
                        subtract(pool, R, n)
                    if n == SQ_AFTER and R.layer1 and R.layer2:
                        low_square(R.r + 1)

            low_square(0)
            rounds(pool, one_round)

        @block.vector
        def _(dve):
            def product(R, n):
                layer, k = R.steps[n]
                used = R.back(n, RING)
                if used:
                    Q, m = used
                    who = KINDS[Q.steps[m]]
                    if who == NATIVE:
                        dve.wait_ge(s_mmhigh, Q.count(m + 1))
                    else:
                        dve.wait_ge(s_low[who], Q.count(m + 1, who))
                if layer == 1:
                    par = 1 - R.parity
                    if k == 0:
                        dve.wait_ge(s_row, 16 * (R.r + 2))
                    t = TILE1[k]
                    dve.wait_ge(s_rot[par][t], R.loads(1))
                    row, x = x_row[:, :], x_rot[:, par, t, :]
                else:
                    if k == 0:
                        dve.wait_ge(s_hidden_ps, R.r + 1)
                    if k == SWAP:
                        dve.wait_ge(s_swapped_ps, R.r + 1)
                    t = TILE2[k]
                    if t not in TILE1 and k < SWAP:
                        dve.wait_ge(s_rot[R.parity][t], R.loads(0))
                    row, x = hidden_ps if k < SWAP else swapped_ps, x_rot[:, R.parity, t, :]
                    row = row[:, :]
                dve.tensor_tensor(z[:, R.slot(n), :], row, x, ALU.mult).then_inc(s_prod, 1)

            def reduce_direct(R):
                dve.wait_ge(s_direct, 2 * (R.r + 1))
                dve.tensor_reduce(sum_direct[:, bass.ds(R.r * (BPC // 2), BPC // 2)],
                                  direct[:, :].rearrange("p (b d) -> p b d", d=DIM), AX_X, ALU.add)\
                   .then_inc(s_red1, 1)

            def reduce_top(R):
                dve.wait_ge(s_top, R.r + 1)
                dve.tensor_reduce(sum_top[:, bass.ds(R.r * BPC, BPC)],
                                  top[:, :].rearrange("p (b d) -> p b d", d=DIM), AX_X, ALU.add)\
                   .then_inc(s_red2, 1)

            def one_round(R):
                for n in range(len(R.steps)):
                    product(R, n)
                    behind = R.back(n, SUB_LAG)
                    if behind and KINDS[behind[0].steps[behind[1]]] == DVE \
                            and (behind[0] is R or behind[0].layer2):
                        subtract(dve, *behind)
                    if R.layer2 and n == RED1_AFTER:
                        reduce_direct(R)
                    if R.layer2 and R.prev.layer2 and n == RED2_AFTER:
                        reduce_top(R.prev)
                if not R.layer2:
                    for n in range(len(R.steps) - SUB_LAG, len(R.steps)):
                        if KINDS[R.steps[n]] == DVE:
                            subtract(dve, R, n)

            dve.wait_ge(s_weights1, 64)
            dve.tensor_tensor(folded_w1, raw_w1a, raw_w1b, ALU.add).then_inc(s_folded, 1)
            dve.wait_ge(s_w1high, W1_HIGH)
            dve.wait_ge(s_folded, 1)
            dve.tensor_tensor(w1l[:, :, :], folded_w1, w1h[:, :, :].bitcast(F32),
                              ALU.subtract).then_inc(s_w1low, 1)
            low = slice(2 * QUAD, 3 * QUAD)
            dve.tensor_tensor(wq[low, :], raw_wsq[low, :], wq[low, :].bitcast(F32),
                              ALU.subtract).then_inc(s_w1low, 1)
            def second_weights():
                dve.wait_ge(s_w2high, W2_HIGH)
                dve.tensor_tensor(w2l[:, :, :], raw_w2[:, :NSPLIT2, :], w2h[:, :, :].bitcast(F32),
                                  ALU.subtract).then_inc(s_w2low, 1)

            last = rounds(dve, one_round, second_weights)
            reduce_top(last)


def kernel(r_cin_inputs, L0_rec_w0, L0_rec_b0, L0_rec_w1, L0_rec_b1):
    import numpy as np
    import concourse.bacc as bacc
    from concourse.bass_utils import run_bass_kernel_spmd

    x = np.asarray(r_cin_inputs)
    rows = np.ascontiguousarray(x.transpose(1, 0, 2)).reshape(FIELD, COLS)
    x2 = rows[np.arange(XROWS) % FIELD].reshape(XROWS, NCHUNK, C).transpose(1, 0, 2)
    x2 = np.ascontiguousarray(x2).reshape(NCHUNK * XROWS, C)

    p = np.arange(P)
    q, i = p // QUAD, p % QUAD
    w0 = np.asarray(L0_rec_w0).reshape(SIZE, FIELD, FIELD)
    t1 = np.arange(1, T1 + 1)
    row_field = np.broadcast_to((i + 4 * q) % FIELD, (T1, P))
    rot_field = (i[None] + t1[:, None] + 8 * q[None]) % FIELD
    w1a = w0[:, row_field, rot_field].transpose(2, 1, 0)
    w1b = w0[:, rot_field, row_field].transpose(2, 1, 0).copy()
    w1b[3 * QUAD:, T1 - 1, :] = 0
    wsq = w0[:, (i + 8 * q) % FIELD, (i + 8 * q) % FIELD].T.copy()
    wsq[3 * QUAD:] = 0
    w1 = np.asarray(L0_rec_w1).reshape(SIZE, HID, FIELD)
    k2 = np.array(SPLIT2 + NATIVE2)[:, None]
    t2 = np.array(TILE2)[k2]
    swap = QUAD * (k2 >= SWAP)
    w2 = w1[:, (p + swap) % HID, (i + t2 + 8 * q) % FIELD]
    w2 = w2.transpose(2, 1, 0)
    bias = np.stack([np.asarray(L0_rec_b0), np.asarray(L0_rec_b1)], axis=1)

    arrays = {"x2": x2, "w1a": w1a, "w1b": w1b, "wsq": wsq, "w2": w2, "bias": bias}
    arrays = {k: np.ascontiguousarray(v) for k, v in arrays.items()}
    nc = bacc.Bacc("TRN2", target_bir_lowering=False, num_devices=1)
    args = [nc.dram_tensor(k, v.shape, mybir.dt.from_np(v.dtype), kind="ExternalInput").ap()
            for k, v in arrays.items()]
    out_direct = nc.dram_tensor("out_direct", (P, BATCH // 2), F32, kind="ExternalOutput").ap()
    out_top = nc.dram_tensor("out_top", (P, BATCH), F32, kind="ExternalOutput").ap()
    build(nc, *args, out_direct, out_top)
    got = run_bass_kernel_spmd(nc, [arrays], core_ids=[0]).results[0]
    direct = np.asarray(got["out_direct"]).reshape(2, HID, NCHUNK, BPC // 2).transpose(2, 0, 3, 1)
    direct = direct.reshape(BATCH, HID)
    return np.ascontiguousarray(np.concatenate([direct, np.asarray(got["out_top"]).T], axis=1))
```
